# Optimizing a Trainium2 kernel written in Bass

```python
import numpy as np
import jax
import jax.numpy as jnp

def _softmax(x, axis=-1):
    return jax.nn.softmax(x, axis=axis)

def _gelu(x):
    return jax.nn.gelu(x, approximate=True)

def _silu(x):
    return jax.nn.silu(x)

def _sigmoid(x):
    return jax.nn.sigmoid(x)

def _layernorm(x, axis=-1, eps=1e-05):
    m = jnp.mean(x, axis=axis, keepdims=True)
    v = jnp.var(x, axis=axis, keepdims=True)
    return (x - m) / jnp.sqrt(v + eps)

def _scatter_add(tgt, idx, src, axis=0):
    return tgt.at[idx].add(src)

def _segment_sum(src, seg, n):
    return jax.ops.segment_sum(src, seg, n)
kernel_name = 'mk_seq_postln_d1_jaxref_r8_2d0934'

def setup_inputs(seed: int=0):
    np.random.seed(seed)
    _w = jnp.asarray

    def _L0_attn_setup():
        import jax, jax.numpy as jnp
        import numpy as np
        import math
        DIM = 128
        NUM_HEADS = 16
        HEAD_DIM = DIM // NUM_HEADS
        SCALE = HEAD_DIM ** (-0.5)
        WINDOW_SIZE = 32
        IS_SLIDING = True
        IS_CAUSAL = True

        def _alibi_slopes(num_heads: int) -> np.ndarray:
            closest_pow2 = 2 ** math.floor(math.log2(num_heads))
            base = 2.0 ** (-2.0 ** (-(math.log2(closest_pow2) - 3)))
            powers = np.arange(1, closest_pow2 + 1, dtype=np.float32)
            slopes = base ** powers
            if num_heads != closest_pow2:
                start = 2.0 ** (-(2.0 ** (-(math.log2(closest_pow2) - 3)) - 1))
                extra = np.linspace(start, base, num_heads - closest_pow2, dtype=np.float32)
                slopes = np.concatenate([slopes, extra])
            return slopes.astype(np.float32)
        key = jax.random.key(seed)
        k_x, k_qw, k_qb, k_pw, k_pb = jax.random.split(key, 5)
        B, N, C = (2, 256, DIM)
        s = C ** (-0.5)
        return {'x': jax.random.normal(k_x, (B, N, C), dtype=jnp.float32), 'qkv_w': jax.random.normal(k_qw, (3 * C, C), dtype=jnp.float32) * s, 'qkv_b': jax.random.normal(k_qb, (3 * C,), dtype=jnp.float32) * 0.02, 'proj_w': jax.random.normal(k_pw, (C, C), dtype=jnp.float32) * s, 'proj_b': jax.random.normal(k_pb, (C,), dtype=jnp.float32) * 0.02}
    _L0_attn_in = _L0_attn_setup()

    def _L0_ffn_setup():
        import jax, jax.numpy as jnp
        import numpy as np
        B, S, D = (2, 256, 128)
        I = 64
        E = 16
        TOP_K = 2

        def _mlp(x, wg, wu, wd):
            return jnp.einsum('bsi,id->bsd', jax.nn.silu(x @ wg) * (x @ wu), wd)
        key = jax.random.key(seed)
        ks = jax.random.split(key, 10)
        sc_d = 1.0 / np.sqrt(D)
        sc_i = 1.0 / np.sqrt(I)
        return {'x': jax.random.normal(ks[0], (B, S, D), dtype=jnp.float32), 'gate_w': jax.random.normal(ks[1], (D, E), dtype=jnp.float32) * sc_d, 'gate_b': jnp.zeros((E,), dtype=jnp.float32), 'shared_wg': jax.random.normal(ks[2], (D, I), dtype=jnp.float32) * sc_d, 'shared_wu': jax.random.normal(ks[3], (D, I), dtype=jnp.float32) * sc_d, 'shared_wd': jax.random.normal(ks[4], (I, D), dtype=jnp.float32) * sc_i, 'experts_wg': jax.random.normal(ks[5], (E, D, I), dtype=jnp.float32) * sc_d, 'experts_wu': jax.random.normal(ks[6], (E, D, I), dtype=jnp.float32) * sc_d, 'experts_wd': jax.random.normal(ks[7], (E, I, D), dtype=jnp.float32) * sc_i}
    _L0_ffn_in = _L0_ffn_setup()
    _d = {'L0_attn_x': _L0_attn_in['x'], 'L0_attn_qkv_w': _L0_attn_in['qkv_w'], 'L0_attn_qkv_b': _L0_attn_in['qkv_b'], 'L0_attn_proj_w': _L0_attn_in['proj_w'], 'L0_attn_proj_b': _L0_attn_in['proj_b'], 'L0_ffn_gate_w': _L0_ffn_in['gate_w'], 'L0_ffn_gate_b': _L0_ffn_in['gate_b'], 'L0_ffn_shared_wg': _L0_ffn_in['shared_wg'], 'L0_ffn_shared_wu': _L0_ffn_in['shared_wu'], 'L0_ffn_shared_wd': _L0_ffn_in['shared_wd'], 'L0_ffn_experts_wg': _L0_ffn_in['experts_wg'], 'L0_ffn_experts_wu': _L0_ffn_in['experts_wu'], 'L0_ffn_experts_wd': _L0_ffn_in['experts_wd']}
    _x0 = _d['L0_attn_x']
    _d['L0_attn_x'] = jax.random.normal(jax.random.fold_in(jax.random.key(seed), 1), (8, 512, 128), dtype=_x0.dtype)
    del _x0
    return _d

def reference(L0_attn_x, L0_attn_qkv_w, L0_attn_qkv_b, L0_attn_proj_w, L0_attn_proj_b, L0_ffn_gate_w, L0_ffn_gate_b, L0_ffn_shared_wg, L0_ffn_shared_wu, L0_ffn_shared_wd, L0_ffn_experts_wg, L0_ffn_experts_wu, L0_ffn_experts_wd):

    def _L0_attn_ref(x, qkv_w, qkv_b, proj_w, proj_b):
        import jax, jax.numpy as jnp
        import numpy as np
        import math
        DIM = 128
        NUM_HEADS = 16
        HEAD_DIM = DIM // NUM_HEADS
        SCALE = HEAD_DIM ** (-0.5)
        WINDOW_SIZE = 32
        IS_SLIDING = True
        IS_CAUSAL = True

        def _alibi_slopes(num_heads: int) -> np.ndarray:
            closest_pow2 = 2 ** math.floor(math.log2(num_heads))
            base = 2.0 ** (-2.0 ** (-(math.log2(closest_pow2) - 3)))
            powers = np.arange(1, closest_pow2 + 1, dtype=np.float32)
            slopes = base ** powers
            if num_heads != closest_pow2:
                start = 2.0 ** (-(2.0 ** (-(math.log2(closest_pow2) - 3)) - 1))
                extra = np.linspace(start, base, num_heads - closest_pow2, dtype=np.float32)
                slopes = np.concatenate([slopes, extra])
            return slopes.astype(np.float32)
        B, N, C = x.shape
        H, D = (NUM_HEADS, HEAD_DIM)
        slopes = jnp.asarray(_alibi_slopes(H))
        qkv = x @ qkv_w.T + qkv_b
        qkv = qkv.reshape(B, N, 3, H, D).transpose(2, 0, 3, 1, 4)
        q, k, v = (qkv[0], qkv[1], qkv[2])
        attn = jnp.einsum('bhnd,bhmd->bhnm', q, k) * SCALE
        pos = jnp.arange(N)
        rel = pos[None, :] - pos[:, None]
        alibi = slopes[:, None, None] * rel.astype(jnp.float32)
        attn = attn + alibi[None]
        if IS_SLIDING:
            attn = jnp.where(jnp.abs(rel) >= WINDOW_SIZE, -jnp.inf, attn)
        if IS_CAUSAL:
            attn = jnp.where(rel > 0, -jnp.inf, attn)
        attn = jax.nn.softmax(attn, axis=-1)
        out = jnp.einsum('bhnm,bhmd->bhnd', attn, v)
        out = out.transpose(0, 2, 1, 3).reshape(B, N, C)
        return out @ proj_w.T + proj_b

    def _L0_ffn_ref(x, gate_w, gate_b, shared_wg, shared_wu, shared_wd, experts_wg, experts_wu, experts_wd):
        import jax, jax.numpy as jnp
        import numpy as np
        B, S, D = (2, 256, 128)
        I = 64
        E = 16
        TOP_K = 2

        def _mlp(x, wg, wu, wd):
            return jnp.einsum('bsi,id->bsd', jax.nn.silu(x @ wg) * (x @ wu), wd)
        router_logits = jax.nn.sigmoid(x @ gate_w + gate_b)
        expert_values, expert_indices = jax.lax.top_k(router_logits, k=TOP_K)
        expert_values = expert_values / jnp.sum(expert_values, axis=-1, keepdims=True)
        hg = jnp.einsum('bsd,edi->bsei', x, experts_wg)
        hu = jnp.einsum('bsd,edi->bsei', x, experts_wu)
        all_outputs = jnp.einsum('bsei,eid->bsed', jax.nn.silu(hg) * hu, experts_wd)
        selected = jnp.take_along_axis(all_outputs, expert_indices[..., None], axis=2)
        expert_weighted = jnp.sum(expert_values[..., None] * selected, axis=2)
        return x + _mlp(x, shared_wg, shared_wu, shared_wd) + expert_weighted
    x = L0_attn_x
    x = _layernorm(x + _L0_attn_ref(x, L0_attn_qkv_w, L0_attn_qkv_b, L0_attn_proj_w, L0_attn_proj_b), axis=-1)
    x = _layernorm(x + _L0_ffn_ref(x, L0_ffn_gate_w, L0_ffn_gate_b, L0_ffn_shared_wg, L0_ffn_shared_wu, L0_ffn_shared_wd, L0_ffn_experts_wg, L0_ffn_experts_wu, L0_ffn_experts_wd), axis=-1)
    return x

_drawn_inputs = setup_inputs


def setup_inputs(seed=0):
    import zlib

    import numpy as np

    out = dict(_drawn_inputs(seed))
    spreads = {'L0_ffn_gate_b': (0.0, 0.1)}
    factors = {}
    for name, (base, spread) in spreads.items():
        noise = np.random.default_rng([zlib.crc32(name.encode()), seed]).standard_normal(out[name].shape)
        drawn = base * np.exp(spread * noise) if base else spread * noise
        out[name] = jnp.asarray(drawn.astype(out[name].dtype))
    for name, factor in factors.items():
        out[name] = (out[name] * factor).astype(out[name].dtype)
    return out
```

```python
from contextlib import ExitStack

import numpy as np
import concourse.bass as bass
from concourse import mybir

F32 = mybir.dt.float32
F32R = mybir.dt.float32r
BF16 = mybir.dt.bfloat16
U32 = mybir.dt.uint32
ALU = mybir.AluOpType
ACT = mybir.ActivationFunctionType
AX = mybir.AxisListType

B, N, C = 8, 512, 128
H, HD = 16, 8
W = 32
G, HG = 4, 4
SB = N // W
T, SBT = N // 128, 128 // W
E, FF = 16, 64
NC_ = E // 2 + 1
EPS = 1e-5
SCALE = HD ** -0.5
MASKED = -1e30
PRODUCTS = (((0, 0), (0, 1), (1, 0), (1, 1)), ((0, 2), (2, 0), (1, 2), (2, 1)))

TURN = [("up", 0), ("route_a",), ("up", 1), ("qk",), ("route_b",), ("v", 0), ("v", 1), ("up", 2),
        ("v", 2), ("v", 3), ("scores", 0), ("down", 0), ("up", 3), ("exp", 0), ("scores", 1),
        ("down", 1), ("up", 4), ("pv", 0), ("exp", 1), ("scores", 2), ("down", 2), ("up", 5),
        ("pv", 1), ("exp", 2), ("scores", 3), ("down", 3), ("up", 6), ("pv", 2), ("exp", 3),
        ("down", 4), ("up", 7), ("pv", 3), ("up", 8), ("down", 5), ("heads_t",), ("down", 6),
        ("proj",), ("down", 7), ("down", 8), ("x1_t",), ("out",)]
FFN_STEPS = ("up", "down", "route_a", "route_b", "out")


def steps(ffn, att):
    return [s for s in TURN if (ffn if s[0] in FFN_STEPS else att)]


def build(nc, x, xt, wqkv_t, qkv_b, wp_t, proj_b, gate_w, gate_b, w_gate, w_up, w_down, w_down_sh,
          ident_in, head_mask_in, pick_in, own_in, prev_in, head_rows_in, ramp_in, out):
    gates_dram = nc.dram_tensor("gates_scratch", [E, N], F32, kind="Internal").ap()
    ctx = ExitStack()
    with ctx:
        def sb(name, shape, dt=F32):
            return ctx.enter_context(nc.sbuf_tensor(name, shape, dt))

        def pb(name, shape):
            return ctx.enter_context(nc.psum_tensor(name, shape, F32))

        def sem(name):
            return ctx.enter_context(nc.semaphore(name))

        ident = sb("ident", [128, 128])
        head_mask = sb("head_mask", [128, 128])
        pick_prev = sb("pick_prev", [128, W], U32)
        alibi_own = sb("alibi_own", [128, G, W])
        alibi_prev = sb("alibi_prev", [128, G, W])
        head_rows = sb("head_rows", [128, HG])
        q_bias = sb("q_bias", [128, 1])
        ramp = sb("ramp", [128, E])
        masked = sb("masked", [128, G, W])
        wqkv = sb("wqkv", [128, 3 * C])
        bqkv = sb("bqkv", [128, 3])
        wp = sb("wp", [128, C])
        pbias = sb("pbias", [128, C])
        gbias = sb("gbias", [E, 1])
        WW = E * FF + FF
        wg_hi, wg_lo = sb("wg_hi", [128, WW], F32R), sb("wg_lo", [128, WW], F32R)
        wu_hi, wu_lo = sb("wu_hi", [128, WW], F32R), sb("wu_lo", [128, WW], F32R)
        gw = sb("gw", [128, E])
        gw_hi, gw_lo = sb("gw_hi", [128, E], F32R), sb("gw_lo", [128, E], F32R)
        wd = sb("wd", [128, E // 2, C])
        wd_sh = sb("wd_sh", [FF, C])

        xin = sb("xin", [128, T, C])
        xtin = sb("xtin", [128, SB, HG, W])
        xb = sb("xb", [128, T, C])
        qk = sb("qk", [128, 2, N])
        rest = sb("rest", [128, 2, N])
        parts = sb("parts", [128, 3, 2, N], BF16)
        q_wide = sb("q_wide", [128, 3, SB, HG, W], BF16)
        q_stack = sb("q_stack", [128, 2, G, SB * HG * W], BF16)
        k_stack = sb("k_stack", [128, 2, G, W + N], BF16)
        vbd = sb("vbd", [128, SB, G, HG, HD + 1])
        sf = sb("sf", [128, 2, G, SBT, W])
        mx = sb("mx", [128, 2, G * SBT])
        px = sb("px", [128, 2, G * SBT * W])
        pt = sb("pt", [128, 2, G, SBT, W])
        p_own = sb("p_own", [128, 2, G, SBT, W])
        p_prev = sb("p_prev", [128, 2, G, SBT, W])
        rden = sb("rden", [128, H])
        on = sb("on", [128, T, H, HD])
        ot = sb("ot", [128, N])
        y1 = sb("y1", [128, T, C])
        x1 = sb("x1", [128, T, C])
        x1r = sb("x1r", [128, T, C])
        xh, xl = sb("xh", [128, N], F32R), sb("xl", [128, N], F32R)
        lt = sb("lt", [E, N])
        rt = sb("rt", [128, 12, T, E])
        rs = sb("rs", [128, 8, T])
        gt = sb("gt", [E, N])
        gate_rows = sb("gate_rows", [128, E // 2, N])
        th = sb("th", [128, 2, N])
        ga = sb("ga", [128, N])
        hid = sb("hid", [128, NC_, N])
        wg, wu = (hid[:, :, :].rearrange("p c n -> p (c n)")[:, n * WW:(n + 1) * WW] for n in range(2))
        stats = sb("stats", [128, T, 6])
        mv = sb("mv", [128, T, 2])
        rstd = sb("rstd", [128, T])
        minus_half = sb("minus_half", [128, T])
        y2 = sb("y2", [128, T, C])
        ob = sb("ob", [128, T, C])

        sc = pb("sc", [128, G, SBT, 2 * W])
        pv = pb("pv", [128, H, HD + 1])
        m0 = pb("m0", [128, N])
        m1 = pb("m1", [128, N])
        pg = pb("pg", [128, N])
        pu = pb("pu", [128, N])
        pd = pb("pd", [128, T, C])

        const_in = sem("const_in")
        const_dve = sem("const_dve")
        const_pool = sem("const_pool")
        const_act = sem("const_act")
        x_in = sem("x_in")
        xb_done = sem("xb_done")
        q_mm, q_out = sem("q_mm"), sem("q_out")
        parts_done = sem("parts_done")
        wide_done = sem("wide_done")
        stack_in = sem("stack_in")
        k_mm, k_out = sem("k_mm"), sem("k_out")
        v_mm, v_out = sem("v_mm"), sem("v_out")
        sc_mm = sem("sc_mm")
        own_out = sem("own_out")
        fold_done = sem("fold_done")
        max_done = sem("max_done")
        sub_done = sem("sub_done")
        exp_done = sem("exp_done")
        pt_done = sem("pt_done")
        own_done = sem("own_done")
        prev_done = sem("prev_done")
        pv_mm = sem("pv_mm")
        rden_done = sem("rden_done")
        on_done = sem("on_done")
        ot_mm, ot_out = sem("ot_mm"), sem("ot_out")
        y_mm, y_out = sem("y_mm"), sem("y_out")
        ln1 = sem("ln1")
        rstd1, rstd2 = sem("rstd1"), sem("rstd2")
        x1t_mm = sem("x1t_mm")
        xh_out, xl_out = sem("xh_out"), sem("xl_out")
        x1r_done = sem("x1r_done")
        lg_mm, lg_out = sem("lg_mm"), sem("lg_out")
        lt_mm, ez_out = sem("lt_mm"), sem("ez_out")
        route = sem("route")
        gt_mm, gt_out = sem("gt_mm"), sem("gt_out")
        gates_out = sem("gates_out")
        gates_in = sem("gates_in")
        up_mm = sem("up_mm")
        tanh_out = sem("tanh_out")
        ga_done = sem("ga_done")
        hid_done = sem("hid_done")
        gated = sem("gated")
        down_mm = sem("down_mm")
        y2_done = sem("y2_done")
        ln2 = sem("ln2")
        out_dma = sem("out_dma")

        STACK = 2 * 2 * 4 * G * 16
        block = ctx.enter_context(nc.Block())

        def apart(eng):
            eng.nop(nofuse=True)

        def turns(eng, work):
            work(None, 0)
            with eng.Fori(0, B - 1) as i:
                work(i, i + 1)
            work(B - 1, None)

        @block.sync
        def _(sp):
            for dst, src in ((ident[:, :], ident_in), (wqkv[:, :], wqkv_t)):
                sp.dma_start(dst, src).then_inc(const_in, 16)

            def load(b):
                sp.dma_start(xtin[:, :, :, :].rearrange("p s h w -> p (s h w)"), xt[b, :, :] if isinstance(b, int) else
                             xt[bass.ds(b, 1), :, :].rearrange("b p n -> (b p) n")).then_inc(x_in, 16)
                sp.dma_start(xin[:, :, :], (x[b, :, :] if isinstance(b, int) else
                             x[bass.ds(b, 1), :, :].rearrange("b n d -> (b n) d"))
                             .rearrange("(t p) d -> p t d", p=128)).then_inc(x_in, 16)

            load(0)
            for dst, src in ((bqkv[:, :], qkv_b),
                             (head_rows[:, :], head_rows_in), (head_mask[:, :], head_mask_in),
                             (pick_prev[:, :], pick_in),
                             (alibi_own[:, :, :], own_in.rearrange("p (g w) -> p g w", g=G)),
                             (alibi_prev[:, :, :], prev_in.rearrange("p (g w) -> p g w", g=G)),
                             (pbias[:, :], proj_b.rearrange("(a n) -> a n", a=1).broadcast_to([128, C])),
                             (wp[:, :], wp_t), (gw[:, :], gate_w), (wg, w_gate), (wu, w_up),
                             (gbias[:, :], gate_b.rearrange("(n a) -> n a", a=1)),
                             (ramp[:, :], ramp_in),
                             (wd[:, :, :], w_down.rearrange("p (c d) -> p c d", d=C)),
                             (wd_sh[:, :], w_down_sh)):
                sp.dma_start(dst, src).then_inc(const_in, 16)

            def spread_gates(b):
                sp.wait_ge(gt_out, b + 1)
                apart(sp)
                if not (isinstance(b, int) and b == 0):
                    sp.wait_ge(gates_in, 32 * b)
                    apart(sp)
                    sp.wait_ge(gated, (NC_ - 1) * b)
                    apart(sp)
                sp.dma_start(gates_dram, gt[:, :]).then_inc(gates_out, 16)
                sp.wait_ge(gates_out, 16 * b + 16)
                apart(sp)
                for e in range(2):
                    sp.dma_start(gate_rows[FF * e:FF * (e + 1), :, :],
                                 gates_dram.rearrange("(c e) n -> e c n", e=2)[e:e + 1, :, :]
                                 .broadcast_to([FF, E // 2, N])).then_inc(gates_in, 16)

            def next_load(b):
                sp.wait_ge(v_mm, 4 * b)
                apart(sp)
                sp.wait_ge(xb_done, b)
                apart(sp)
                load(b)

            def store(b):
                sp.wait_ge(ln2, 4 * b + 4)
                apart(sp)
                sp.dma_start((out[b, :, :] if isinstance(b, int) else
                              out[bass.ds(b, 1), :, :].rearrange("b n d -> (b n) d"))
                             .rearrange("(t p) d -> p t d", p=128), ob[:, :, :]).then_inc(out_dma, 16)

            def stack(b):
                sp.wait_ge(wide_done, b + 1)
                apart(sp)
                if not (isinstance(b, int) and b == 0):
                    sp.wait_ge(sc_mm, 4 * b)
                    apart(sp)
                for a in range(2):
                    for n, (qp, kp) in enumerate(PRODUCTS[a]):
                        for g in range(G):
                            dst, src = slice(32 * n, 32 * n + 32), slice(32 * g, 32 * g + 32)
                            sp.dma_start(k_stack[dst, a, g, W:], parts[src, kp, 1, :]).then_inc(stack_in, 16)
                            sp.dma_start(q_stack[dst, a, g, :], q_wide[src, qp].rearrange("p s h w -> p (s h w)"))\
                                .then_inc(stack_in, 16)

            stack(0)
            next_load(1)
            spread_gates(0)
            stack(1)
            next_load(2)
            with sp.Fori(1, B - 2) as i:
                store(i - 1)
                spread_gates(i)
                stack(i + 1)
                next_load(i + 2)
            store(B - 3)
            spread_gates(B - 2)
            stack(B - 1)
            store(B - 2)
            spread_gates(B - 1)
            store(B - 1)
            sp.wait_ge(out_dma, 16 * B)
            apart(sp)

        @block.gpsimd
        def _(pool):
            pool.memset(masked[:, :, :], MASKED).then_inc(const_pool, 1)
            pool.memset(k_stack[:, :, :, 0:W], 0.0).then_inc(const_pool, 1)
            pool.memset(vbd[:, :, :, :, HD:HD + 1], 1.0).then_inc(const_pool, 1)
            pool.memset(minus_half[:, :], -0.5).then_inc(const_pool, 1)
            pool.wait_ge(const_pool, 4)
            pool.wait_ge(const_in, 16 * 17)
            for h in range(HG):
                pool.tensor_copy(vbd[:, :, :, h, HD:HD + 1].rearrange("p s g a -> p (s g) a"),
                                 head_mask[:, h * HD:h * HD + 1].rearrange("p (s a) -> p s a", s=1)
                                 .broadcast_to([128, SB * G, 1])).then_inc(const_pool, 1)

            def work(bf, ba):
                for step in steps(bf is not None, ba is not None):
                    first = isinstance(ba, int) and ba == 0
                    if step[0] == "qk":
                        pool.wait_ge(x_in, 32 * ba + 32)
                        if not first:
                            pool.wait_ge(y_out, ba)
                        pool.tensor_tensor(xb[:, :, :], xin[:, :, :],
                                           pbias[:, :].rearrange("p (a d) -> p a d", a=1).broadcast_to([128, T, C]),
                                           ALU.add).then_inc(xb_done, 1)
                    elif step[0] == "exp":
                        t = step[1]
                        pool.wait_ge(pt_done, 4 * ba + t + 1)
                        if not (first and t < 2):
                            pool.wait_ge(pv_mm, 4 * ba + t - 1)
                        pool.tensor_tensor(p_prev[:, t % 2], pt[:, t % 2],
                                           alibi_prev[:, :, :].rearrange("p g (a w) -> p g a w", a=1)
                                           .broadcast_to([128, G, SBT, W]), ALU.mult).then_inc(prev_done, 1)
                    elif step[0] == "route_a":
                        pool.wait_ge(ln1, 4 * bf + 4)
                        if not (isinstance(bf, int) and bf == 0):
                            pool.wait_ge(y2_done, bf)
                        apart(pool)
                        pool.tensor_copy(x1r[:, :, :], x1[:, :, :]).then_inc(x1r_done, 1)
                    elif step[0] == "up" and step[1] > 0:
                        j = step[1]
                        pool.wait_ge(gates_in, 32 * bf + 32)
                        pool.wait_ge(hid_done, NC_ * bf + j + 1)
                        pool.tensor_tensor(hid[:, j, :], hid[:, j, :], gate_rows[:, j - 1, :],
                                           ALU.mult).then_inc(gated, 1)

                    elif step[0] in ("proj", "out"):
                        s, done, b = (ln1, rstd1, ba) if step[0] == "proj" else (ln2, rstd2, bf)
                        pool.wait_ge(s, 4 * b + 3)
                        pool.tensor_tensor(rstd[:, :], rstd[:, :], minus_half[:, :], ALU.pow).then_inc(done, 1)

            turns(pool, work)

        @block.scalar
        def _(act):
            act.wait_ge(const_in, 16 * 17)
            act.activation(wg_hi[:, :], wg, ACT.Copy).then_inc(const_act, 1)
            act.activation(wu_hi[:, :], wu, ACT.Copy).then_inc(const_act, 1)
            act.activation(gw_hi[:, :], gw[:, :], ACT.Copy).then_inc(const_act, 1)
            act.wait_ge(const_dve, 1)

            def work(bf, ba):
                for step in steps(bf is not None, ba is not None):
                    first = isinstance(ba, int) and ba == 0
                    kind = step[0]
                    if kind == "up":
                        j = step[1]
                        rows = FF if j == 0 else 128
                        act.wait_ge(up_mm, NC_ * bf + j + 1)
                        act.activation(th[0:rows, j % 2, :], pg[0:rows, :], ACT.Tanh, scale=0.5).then_inc(tanh_out, 1)
                    elif kind == "route_a":
                        act.wait_ge(lg_mm, bf + 1)
                        act.activation(lt[:, :], m1[0:E, :], ACT.Identity, bias=gbias[:, 0:1]).then_inc(lg_out, 1)
                        act.wait_ge(lt_mm, bf + 1)
                        act.activation(rt[:, 0, :, :].rearrange("p t e -> p (t e)"), m0[:, 0:T * E], ACT.Exp,
                                       scale=-1.0).then_inc(ez_out, 1)
                    elif kind == "route_b":
                        act.wait_ge(gt_mm, bf + 1)
                        if not (isinstance(bf, int) and bf == 0):
                            act.wait_ge(gates_out, 16 * bf)
                        act.activation(gt[:, :], m1[0:E, :], ACT.Copy).then_inc(gt_out, 1)
                    elif kind == "qk":
                        act.wait_ge(q_mm, ba + 1)
                        if not first:
                            act.wait_ge(parts_done, 4 * ba)
                        act.activation(qk[:, 0, :], m0[:, :], ACT.Identity, bias=q_bias[:, 0:1],
                                       scale=SCALE).then_inc(q_out, 1)
                        act.wait_ge(k_mm, ba + 1)
                        act.activation(qk[:, 1, :], m1[:, :], ACT.Identity, bias=bqkv[:, 1:2]).then_inc(k_out, 1)
                    elif kind == "scores":
                        t = step[1]
                        act.wait_ge(sc_mm, 4 * ba + t + 1)
                        act.activation(sf[:, t % 2], sc[:, :, :, W:2 * W], ACT.Copy).then_inc(own_out, 1)
                    elif kind == "exp":
                        t = step[1]
                        act.wait_ge(sub_done, 4 * ba + t + 1)
                        act.activation(px[:, t % 2, :], sf[:, t % 2].rearrange("p g s w -> p (g s w)"),
                                       ACT.Exp).then_inc(exp_done, 1)
                    elif kind == "heads_t":
                        act.wait_ge(ot_mm, ba + 1)
                        act.activation(ot[:, :], m0[:, :], ACT.Identity, bias=bqkv[:, 2:3]).then_inc(ot_out, 1)
                    elif kind == "x1_t":
                        act.wait_ge(x1t_mm, ba + 1)
                        act.activation(xh[:, :], m0[:, :], ACT.Copy).then_inc(xh_out, 1)

            turns(act, work)

        @block.vector
        def _(dve):
            dve.wait_ge(const_in, 16 * 17)
            dve.tensor_scalar(q_bias[:, :], bqkv[:, 0:1], SCALE, None, ALU.mult).then_inc(const_dve, 1)
            dve.wait_ge(const_act, 3)
            for lo, w, hi in ((wg_lo, wg, wg_hi), (wu_lo, wu, wu_hi), (gw_lo, gw[:, :], gw_hi)):
                dve.tensor_tensor(lo[:, :], w, hi[:, :].bitcast(F32), ALU.subtract).then_inc(const_dve, 1)
            dve.wait_ge(const_pool, 1)

            def chain(s, per, b):
                done = [0]

                def link(ins, alone=False):
                    done[0] += 1
                    ins.then_inc(s, 1)
                    dve.wait_ge(s, per * b + done[0])
                    if alone:
                        apart(dve)
                return link

            def layer_norm(s, rs_done, src, dst, b):
                link = chain(s, 4, b)
                for t in range(T):
                    last = dve.bn_stats(stats[:, t, :], src[:, t, :])
                link(last, alone=True)
                for t in range(T):
                    last = dve.bn_aggr(mv[:, t, :], stats[:, t, :])
                link(last)
                link(dve.tensor_scalar(rstd[:, :], mv[:, :, 1], EPS, None, ALU.add))
                dve.wait_ge(rs_done, b + 1)
                for t in range(T):
                    last = dve.tensor_scalar(dst[:, t, :], src[:, t, :], mv[:, t, 0:1], rstd[:, t:t + 1],
                                             ALU.subtract, ALU.mult)
                link(last)

            def per_token(v):
                return v.rearrange("p (t a) -> p t a", a=1).broadcast_to([128, T, E])

            def router(b):
                link = chain(route, 16, b)
                e, v, eq, key, s1, v2, s2, sel, gates = (rt[:, n] for n in range(9))
                m1_, k1, m2, k2, den, rd = (rs[:, n] for n in range(6))
                ramps = ramp[:, :].rearrange("p (a e) -> p a e", a=1).broadcast_to([128, T, E])
                link(dve.tensor_scalar(e, e, 1.0, None, ALU.add))
                link(dve.reciprocal(v, e))

                def pick(val, top, kmax, chosen):
                    link(dve.tensor_reduce(top, val, AX.X, ALU.max))
                    link(dve.tensor_tensor(eq, val, per_token(top), ALU.is_equal))
                    link(dve.tensor_tensor(key, eq, ramps, ALU.mult))
                    link(dve.tensor_reduce(kmax, key, AX.X, ALU.max))
                    link(dve.tensor_tensor(chosen, key, per_token(kmax), ALU.is_equal))

                pick(v, m1_, k1, s1)
                link(dve.scalar_tensor_tensor(out=v2, in0=s1, scalar=-2.0, in1=v, op0=ALU.mult, op1=ALU.add))
                pick(v2, m2, k2, s2)
                dve.tensor_tensor(den, m1_, m2, ALU.add)
                link(dve.tensor_tensor(sel, s1, s2, ALU.add))
                dve.reciprocal(rd, den)
                link(dve.tensor_tensor(eq, sel, v, ALU.mult))
                link(dve.tensor_tensor(gates, eq, per_token(rd), ALU.mult))

            def work(bf, ba):
                for step in steps(bf is not None, ba is not None):
                    first = isinstance(ba, int) and ba == 0
                    kind = step[0]
                    if kind == "up":
                        j = step[1]
                        rows = FF if j == 0 else 128
                        dve.wait_ge(tanh_out, NC_ * bf + j + 1)
                        dve.scalar_tensor_tensor(out=ga[0:rows, :], in0=th[0:rows, j % 2, :], scalar=1.0,
                                                 in1=pg[0:rows, :], op0=ALU.add, op1=ALU.mult).then_inc(ga_done, 1)
                        dve.wait_ge(ga_done, NC_ * bf + j + 1)
                        dve.scalar_tensor_tensor(out=hid[0:rows, j, :], in0=ga[0:rows, :], scalar=0.5,
                                                 in1=pu[0:rows, :], op0=ALU.mult, op1=ALU.mult).then_inc(hid_done, 1)
                    elif kind == "route_a":
                        dve.wait_ge(ez_out, bf + 1)
                        router(bf)
                    elif kind == "qk":
                        dve.wait_ge(q_out, ba + 1)
                        dve.wait_ge(k_out, ba + 1)
                        if not first:
                            dve.wait_ge(stack_in, STACK * ba)
                        link = chain(parts_done, 4, ba)
                        link(dve.tensor_copy(parts[:, 0], qk[:, :, :]))
                        link(dve.tensor_tensor(rest[:, :, :], qk[:, :, :], parts[:, 0], ALU.subtract))
                        link(dve.tensor_copy(parts[:, 1], rest[:, :, :]))
                        link(dve.tensor_tensor(parts[:, 2], rest[:, :, :], parts[:, 1], ALU.subtract))
                        for n in range(3):
                            for h in range(HG):
                                last = dve.tensor_scalar(q_wide[:, n, :, h, :],
                                                         parts[:, n, 0, :].rearrange("p (s w) -> p s w", w=W),
                                                         head_rows[:, h:h + 1], None, ALU.mult)
                        last.then_inc(wide_done, 1)
                    elif kind == "v":
                        r = step[1]
                        dve.wait_ge(v_mm, 4 * ba + r + 1)
                        m = (m0, m1)[r % 2]
                        dve.tensor_tensor(vbd[:, SBT * r:SBT * (r + 1), :, :, 0:HD].rearrange("p s g h d -> p (s g h) d"),
                                          m[:, :].rearrange("p (a d) -> p a d", d=HD),
                                          head4[:, :].rearrange("p (a d) -> p a d", d=HD), ALU.mult).then_inc(v_out, 1)
                    elif kind == "scores":
                        t = step[1]
                        dve.wait_ge(own_out, 4 * ba + t + 1)
                        apart(dve)
                        picks = pick_prev[:, :].rearrange("p (a c w) -> p a c w", a=1, c=1)
                        s0 = 1 if t == 0 else 0
                        if t == 0:
                            dve.copy_predicated(sf[:, 0, :, 0, :],
                                                pick_prev[:, :].rearrange("p (a w) -> p a w", a=1).broadcast_to([128, G, W]),
                                                masked[:, :, :])
                        dve.copy_predicated(sf[:, t % 2, :, s0:SBT, :], picks.broadcast_to([128, G, SBT - s0, W]),
                                            sc[:, :, s0:SBT, 0:W]).then_inc(fold_done, 1)
                        dve.wait_ge(fold_done, 4 * ba + t + 1)
                        flat = sf[:, t % 2].rearrange("p g s w -> p (g s) w")
                        dve.tensor_reduce(mx[:, t % 2, :], flat, AX.X, ALU.max).then_inc(max_done, 1)
                        dve.wait_ge(max_done, 4 * ba + t + 1)
                        dve.tensor_tensor(flat, flat, mx[:, t % 2, :].rearrange("p (a w) -> p a w", w=1)
                                          .broadcast_to([128, G * SBT, W]), ALU.subtract).then_inc(sub_done, 1)
                    elif kind == "exp":
                        t = step[1]
                        dve.wait_ge(exp_done, 4 * ba + t + 1)
                        if not (first and t < 2):
                            dve.wait_ge(prev_done, 4 * ba + t - 1)
                        dve.transpose(pt[:, t % 2].rearrange("p g s w -> p (g s w)"), px[:, t % 2, :]).then_inc(pt_done, 1)
                        dve.wait_ge(pt_done, 4 * ba + t + 1)
                        if not (first and t < 2):
                            dve.wait_ge(pv_mm, 4 * ba + t - 1)
                        dve.tensor_tensor(p_own[:, t % 2], pt[:, t % 2],
                                          alibi_own[:, :, :].rearrange("p g (a w) -> p g a w", a=1)
                                          .broadcast_to([128, G, SBT, W]), ALU.mult).then_inc(own_done, 1)
                    elif kind == "pv":
                        t = step[1]
                        dve.wait_ge(pv_mm, 4 * ba + t + 1)
                        dve.reciprocal(rden[:, :], pv[:, :, HD]).then_inc(rden_done, 1)
                        dve.wait_ge(rden_done, 4 * ba + t + 1)
                        dve.tensor_tensor(on[:, t, :, :], pv[:, :, 0:HD],
                                          rden[:, :].rearrange("p (h a) -> p h a", a=1).broadcast_to([128, H, HD]),
                                          ALU.mult).then_inc(on_done, 1)
                    elif kind == "proj":
                        dve.wait_ge(y_mm, ba + 1)
                        dve.wait_ge(xb_done, ba + 1)
                        dve.tensor_tensor(y1[:, :, :], m1[:, :].rearrange("p (t d) -> p t d", t=T), xb[:, :, :],
                                          ALU.add).then_inc(y_out, 1)
                        dve.wait_ge(y_out, ba + 1)
                        if not first:
                            dve.wait_ge(x1r_done, ba)
                        layer_norm(ln1, rstd1, y1, x1, ba)
                    elif kind == "x1_t":
                        dve.wait_ge(xh_out, ba + 1)
                        dve.tensor_tensor(xl[:, :], m0[:, :], xh[:, :].bitcast(F32), ALU.subtract).then_inc(xl_out, 1)
                    elif kind == "out":
                        dve.wait_ge(down_mm, NC_ * bf + NC_)
                        dve.wait_ge(x1r_done, bf + 1)
                        dve.scalar_tensor_tensor(out=y2[:, :, :], in0=x1r[:, :, :], scalar=2.0, in1=pd[:, :, :],
                                                 op0=ALU.mult, op1=ALU.add).then_inc(y2_done, 1)
                        dve.wait_ge(y2_done, bf + 1)
                        if not (isinstance(bf, int) and bf == 0):
                            dve.wait_ge(out_dma, 16 * bf)
                        layer_norm(ln2, rstd2, y2, ob, bf)

            head4 = sb("head4", [128, SBT * 128])
            for s in range(SBT):
                last = dve.tensor_copy(head4[:, 128 * s:128 * (s + 1)], head_mask[:, :])
            last.then_inc(const_dve, 1)
            dve.wait_ge(const_dve, 5)
            turns(dve, work)

        @block.tensor
        def _(pe):
            pe.wait_ge(const_in, 16 * 17)
            pe.wait_ge(const_pool, 8)
            pe.wait_ge(const_act, 3)
            pe.wait_ge(const_dve, 5)

            def split_matmul(dst, w_hi, w_lo, start=True, stop=True):
                pe.matmul(dst, w_hi, xh[:, :], start=True, stop=False)
                pe.matmul(dst, w_hi, xl[:, :], start=False, stop=False)
                return pe.matmul(dst, w_lo, xh[:, :], start=False, stop=True)

            def work(bf, ba):
                for step in steps(bf is not None, ba is not None):
                    first = isinstance(ba, int) and ba == 0
                    kind = step[0]
                    if kind == "up":
                        j = step[1]
                        pe.wait_ge(xh_out, bf + 1)
                        pe.wait_ge(xl_out, bf + 1)
                        if not (isinstance(bf, int) and bf == 0 and j == 0):
                            pe.wait_ge(hid_done, NC_ * bf + j)
                        c0, c1 = (E * FF, E * FF + FF) if j == 0 else (128 * (j - 1), 128 * j)
                        split_matmul(pg[0:c1 - c0, :], wg_hi[:, c0:c1], wg_lo[:, c0:c1])
                        split_matmul(pu[0:c1 - c0, :], wu_hi[:, c0:c1], wu_lo[:, c0:c1]).then_inc(up_mm, 1)
                    elif kind == "down":
                        j = step[1]
                        if j == 0:
                            pe.wait_ge(hid_done, NC_ * bf + 1)
                            if not (isinstance(bf, int) and bf == 0):
                                pe.wait_ge(y2_done, bf)
                        else:
                            pe.wait_ge(gated, (NC_ - 1) * bf + j)
                        rows = FF if j == 0 else 128
                        for t in range(T):
                            last = pe.matmul(pd[:, t, :], hid[0:rows, j, 128 * t:128 * (t + 1)],
                                             wd_sh[:, :] if j == 0 else wd[:, j - 1, :],
                                             start=(j == 0 and t == 0), stop=(j == NC_ - 1), skip_group_check=True)
                        last.then_inc(down_mm, 1)
                    elif kind == "route_a":
                        split_matmul(m1[0:E, :], gw_hi[:, :], gw_lo[:, :]).then_inc(lg_mm, 1)
                        pe.wait_ge(lg_out, bf + 1)
                        apart(pe)
                        for t in range(T):
                            last = pe.transpose(m0[:, E * t:E * (t + 1)], lt[:, 128 * t:128 * (t + 1)], ident[0:E, 0:E])
                        last.then_inc(lt_mm, 1)
                    elif kind == "route_b":
                        pe.wait_ge(route, 16 * bf + 16)
                        if ba is not None:
                            pe.wait_ge(k_out, ba + 1)
                        for t in range(T):
                            last = pe.transpose(m1[0:E, 128 * t:128 * (t + 1)], rt[:, 8, t, :], ident[:, :])
                        last.then_inc(gt_mm, 1)
                    elif kind == "qk":
                        pe.wait_ge(x_in, 32 * ba + 32)
                        if bf is not None:
                            pe.wait_ge(ez_out, bf + 1)
                        pe.matmul(m0[:, :], wqkv[:, 0:C], xtin[:, :, 0, :], start=True, stop=True).then_inc(q_mm, 1)
                        pe.matmul(m1[:, :], wqkv[:, C:2 * C], xtin[:, :, 0, :], start=True, stop=True).then_inc(k_mm, 1)
                    elif kind == "v":
                        r = step[1]
                        if r == 0:
                            pe.wait_ge(q_out, ba + 1)
                        elif r == 1:
                            pe.wait_ge(k_out, ba + 1)
                            if bf is not None:
                                pe.wait_ge(gt_out, bf + 1)
                        else:
                            pe.wait_ge(v_out, 4 * ba + r - 1)
                        for s in range(SBT):
                            last = pe.matmul((m0, m1)[r % 2][:, 128 * s:128 * (s + 1)],
                                             xtin[:, SBT * r + s].rearrange("p h w -> p (h w)"),
                                             wqkv[:, 2 * C:3 * C], start=True, stop=True)
                        last.then_inc(v_mm, 1)
                    elif kind == "scores":
                        t = step[1]
                        pe.wait_ge(stack_in, STACK * ba + STACK)
                        if not (first and t == 0):
                            pe.wait_ge(fold_done, 4 * ba + t)
                        for g in range(G):
                            for s in range(SBT):
                                n = SBT * t + s
                                for a in range(2):
                                    last = pe.matmul(sc[:, g, s, :], q_stack[:, a, g, 128 * n:128 * (n + 1)],
                                                     k_stack[:, a, g, W * n:W * (n + 2)],
                                                     start=(a == 0), stop=(a == 1))
                        last.then_inc(sc_mm, 1)
                    elif kind == "pv":
                        t = step[1]
                        pe.wait_ge(own_done, 4 * ba + t + 1)
                        pe.wait_ge(prev_done, 4 * ba + t + 1)
                        if t == 0:
                            pe.wait_ge(v_out, 4 * ba + 4)
                        if not (first and t == 0):
                            pe.wait_ge(on_done, 4 * ba + t)
                        for s in range(SBT):
                            b_ = SBT * t + s
                            for g in range(G):
                                dst = pv[W * s:W * (s + 1), HG * g:HG * (g + 1), :].rearrange("p h d -> p (h d)")
                                last = pe.matmul(dst, p_own[:, t % 2, g, s, :],
                                                 vbd[:, b_, g].rearrange("p h d -> p (h d)"),
                                                 start=True, stop=(b_ == 0), tile_position=(0, W * s))
                                if b_ > 0:
                                    last = pe.matmul(dst, p_prev[:, t % 2, g, s, :],
                                                     vbd[:, b_ - 1, g].rearrange("p h d -> p (h d)"),
                                                     start=False, stop=True, tile_position=(0, W * s))
                        last.then_inc(pv_mm, 1)
                    elif kind == "heads_t":
                        pe.wait_ge(on_done, 4 * ba + 4)
                        for t in range(T):
                            last = pe.transpose(m0[:, 128 * t:128 * (t + 1)],
                                                on[:, t].rearrange("p h d -> p (h d)"), ident[:, :])
                        last.then_inc(ot_mm, 1)
                    elif kind == "proj":
                        pe.wait_ge(ot_out, ba + 1)
                        for t in range(T):
                            last = pe.matmul(m1[:, 128 * t:128 * (t + 1)], ot[:, 128 * t:128 * (t + 1)], wp[:, :],
                                             start=True, stop=True)
                        last.then_inc(y_mm, 1)
                    elif kind == "x1_t":
                        pe.wait_ge(ln1, 4 * ba + 4)
                        for t in range(T):
                            last = pe.transpose(m0[:, 128 * t:128 * (t + 1)], x1[:, t, :], ident[:, :])
                        last.then_inc(x1t_mm, 1)

            turns(pe, work)


def constants():
    p = np.arange(128)
    ident = np.eye(128, dtype=np.float32)
    cols = np.arange(128)
    head_mask = ((p[:, None] // W) == (cols[None, :] // HD) % HG).astype(np.float32)
    pick = (np.arange(W)[None, :] > (p[:, None] % W)).astype(np.uint32)
    slopes = (2.0 ** -0.5) ** np.arange(1, H + 1)
    head = np.arange(G)[None, :, None] * HG + (p // W)[:, None, None]
    key = (p % W)[:, None, None]
    q = np.arange(W)[None, None, :]
    own = np.where(key <= q, np.exp(slopes[head] * (key - q)), 0.0)
    prev = np.where(key > q, np.exp(slopes[head] * (key - W - q)), 0.0)
    head_rows = (p[:, None] // HD) % HG == np.arange(HG)[None, :]
    ramp = np.broadcast_to(E - np.arange(E, dtype=np.float32), (128, E))
    f = lambda a: np.ascontiguousarray(a.reshape(128, -1).astype(np.float32))
    return dict(ident=ident, head_mask=head_mask, pick=pick, own=f(own), prev=f(prev), head_rows=f(head_rows), ramp=f(ramp))


def kernel(**inputs):
    import concourse.bacc as bacc
    from concourse.bass_utils import run_bass_kernel_spmd

    a = {k.replace("L0_", ""): np.asarray(v) for k, v in inputs.items()}
    c = np.ascontiguousarray

    def experts(routed, shared):
        return c(np.concatenate([routed.transpose(1, 0, 2).reshape(C, E * FF), shared], axis=1))

    data = dict(
        x=c(a["attn_x"]), xt=c(np.broadcast_to(a["attn_x"].transpose(0, 2, 1).reshape(B, C, SB, 1, W), (B, C, SB, HG, W))
             .reshape(B, C, -1)), wqkv_t=c(a["attn_qkv_w"].T),
        qkv_b=c(a["attn_qkv_b"].reshape(3, C).T), wp_t=c(a["attn_proj_w"].T), proj_b=c(a["attn_proj_b"]),
        gate_w=c(a["ffn_gate_w"]), gate_b=c(a["ffn_gate_b"]),
        w_gate=experts(a["ffn_experts_wg"], a["ffn_shared_wg"]),
        w_up=experts(a["ffn_experts_wu"], a["ffn_shared_wu"]),
        w_down=c(a["ffn_experts_wd"].reshape(E // 2, 128, C).transpose(1, 0, 2).reshape(128, -1)),
        w_down_sh=c(a["ffn_shared_wd"]))
    data.update(constants())

    nc = bacc.Bacc("TRN2", target_bir_lowering=False, num_devices=1)
    args = [nc.dram_tensor("in_" + k, v.shape, mybir.dt.from_np(v.dtype), kind="ExternalInput").ap()
            for k, v in data.items()]
    args.append(nc.dram_tensor("out", [B, N, C], F32, kind="ExternalOutput").ap())
    build(nc, *args)
    r = run_bass_kernel_spmd(nc, [{"in_" + k: v for k, v in data.items()}], core_ids=[0])
    return r.results[0]["out"]
```

```python
from contextlib import ExitStack

import numpy as np
import concourse.bass as bass
from concourse import mybir

F32 = mybir.dt.float32
F32R = mybir.dt.float32r
BF16 = mybir.dt.bfloat16
U32 = mybir.dt.uint32
ALU = mybir.AluOpType
ACT = mybir.ActivationFunctionType
AX = mybir.AxisListType

B, N, C = 8, 512, 128
H, HD = 16, 8
W = 32
G, HG = 4, 4
SB = N // W
T, SBT = N // 128, 128 // W
E, FF = 16, 64
NC_ = E // 2 + 1
EPS = 1e-5
SCALE = HD ** -0.5
MASKED = -1e30
PARTS = 3
ROWS = PARTS * PARTS * HD

LATE = 5
TURN = dict(
    PE=[("scores", 0), ("logits",), ("down", 5), ("logits_t",), ("gate_w", 0), ("qk",), ("down", 6), ("up", 0),
        ("scores", 1), ("pv", 0), ("gate_w", 1), ("down", 7), ("down", 8), ("up", 1), ("gates_t",),
        ("gate_w", 2), ("scores", 2), ("up", 2), ("gate_w", 3), ("pv", 1), ("scores", 3), ("gate_w", 4),
        ("up", 3), ("down", 0), ("up", 4), ("gate_w", 5), ("pv", 2), ("up", 5), ("down", 1), ("gate_w", 6),
        ("up", 6), ("pv", 3), ("gate_w", 7), ("heads_t",), ("down", 2), ("proj",), ("gate_w", 8), ("up", 7),
        ("v",), ("down", 3), ("down", 4), ("up", 8), ("x1_t",)],
    ACT=[("scores", 0), ("logits",), ("logits_t",), ("silu", 0), ("exp", 0), ("scores", 1), ("qk",),
        ("silu", 1), ("part0",), ("exp", 1), ("silu", 2), ("gates_t",), ("scores", 2), ("silu", 3), ("keep",),
        ("split",), ("exp", 2), ("silu", 4), ("scores", 3), ("silu", 5), ("exp", 3), ("silu", 6), ("silu", 7),
        ("heads_t",), ("silu", 8), ("store",), ("v", 0), ("v", 1), ("v", 2), ("x1_t",), ("v", 3)],
    DVE=[("scores", 0), ("router", 0), ("router", 1), ("exp", 0), ("silu", 0), ("router", 2), ("up", 0),
        ("scores", 1), ("router", 3), ("silu", 1), ("pv", 0), ("up", 1), ("exp", 1), ("silu", 2),
        ("residual",), ("scores", 2), ("up", 2), ("silu", 3), ("pv", 1), ("exp", 2), ("up", 3), ("silu", 4),
        ("scores", 3), ("up", 4), ("silu", 5), ("up", 5), ("exp", 3), ("pv", 2), ("silu", 6), ("up", 6),
        ("pv", 3), ("norm",), ("silu", 7), ("proj",), ("up", 7), ("x1",), ("silu", 8), ("up", 8), ("x1_t",)],
    POOL=[("scores", 0), ("exp", 0), ("scores", 1), ("part0",), ("exp", 1), ("scores", 2), ("split",),
        ("exp", 2), ("gate", 1), ("scores", 3), ("gate", 2), ("exp", 3), ("gate", 3), ("norm",), ("gate", 4),
        ("proj",), ("xb",), ("gate", 5), ("gate", 6), ("gate", 7), ("gate", 8)],
)
FILL = dict(
    PE=[("qk",), ("scores", 0), ("scores", 1), ("pv", 0), ("scores", 2), ("pv", 1), ("scores", 3), ("pv", 2),
        ("pv", 3), ("heads_t",), ("proj",), ("v",), ("x1_t",)],
    ACT=[("scores", 0), ("exp", 0), ("scores", 1), ("qk",), ("exp", 1), ("part0",), ("scores", 2), ("split",),
        ("exp", 2), ("scores", 3), ("exp", 3), ("heads_t",), ("v", 0), ("v", 1), ("v", 2), ("x1_t",), ("v", 3)],
    DVE=[("scores", 0), ("exp", 0), ("scores", 1), ("pv", 0), ("exp", 1), ("scores", 2), ("exp", 2),
        ("scores", 3), ("pv", 1), ("exp", 3), ("pv", 2), ("pv", 3), ("proj",), ("x1",), ("x1_t",)],
    POOL=[("scores", 0), ("exp", 0), ("scores", 1), ("exp", 1), ("part0",), ("scores", 2), ("split",),
        ("exp", 2), ("scores", 3), ("exp", 3), ("proj",), ("xb",)],
)
DRAIN = dict(
    PE=[("logits",), ("gate_w", 0), ("logits_t",), ("down", 5), ("up", 0), ("down", 6), ("gate_w", 1),
        ("up", 1), ("gate_w", 2), ("gates_t",), ("up", 2), ("gate_w", 3), ("down", 7), ("up", 3),
        ("gate_w", 4), ("down", 8), ("gate_w", 5), ("up", 4), ("up", 5), ("gate_w", 6), ("up", 6), ("down", 0),
        ("down", 1), ("gate_w", 7), ("down", 2), ("up", 7), ("gate_w", 8), ("down", 3), ("down", 4), ("up", 8)],
    ACT=[("logits",), ("logits_t",), ("silu", 0), ("silu", 1), ("silu", 2), ("gates_t",), ("silu", 3),
        ("silu", 4), ("silu", 5), ("silu", 6), ("keep",), ("silu", 7), ("store",), ("silu", 8)],
    DVE=[("router", 0), ("router", 1), ("silu", 0), ("router", 2), ("up", 0), ("silu", 1), ("router", 3),
        ("up", 1), ("silu", 2), ("up", 2), ("silu", 3), ("up", 3), ("silu", 4), ("silu", 5), ("up", 4),
        ("up", 5), ("residual",), ("silu", 6), ("norm",), ("up", 6), ("silu", 7), ("up", 7), ("silu", 8),
        ("up", 8)],
    POOL=[("gate", 1), ("gate", 2), ("gate", 3), ("gate", 4), ("norm",), ("gate", 5), ("gate", 6), ("gate", 7),
        ("gate", 8)],
)
OUT_STEPS = ("residual", "norm", "store")
FFN_STEPS = ("gate_w", "silu", "up", "gate", "down", "logits", "logits_t", "router", "gates_t", "keep")
PRE_STEPS = ("qk", "part0", "split", "v", "xb")


def steps(engine, out, ffn, att, pre):
    order = (FILL if out is None and ffn is None else DRAIN if att is None else TURN)[engine]
    late = lambda s: s[0] == "down" and s[1] >= LATE
    return [s for s in order if (out if s[0] in OUT_STEPS or late(s) else ffn if s[0] in FFN_STEPS else
                                 pre if s[0] in PRE_STEPS else att) is not None]


def build(nc, x, xt, wqkv_t, qkv_b, wp_t, proj_b, gate_w, gate_b, w_gate, w_up, w_down, w_down_sh,
          ident_in, pick_in, own_in, prev_in, ramp_in, out):
    gates_dram = nc.dram_tensor("gates_scratch", [E, N], F32, kind="Internal").ap()
    q_dram = nc.dram_tensor("q_parts", [PARTS, HD * H, N], BF16, kind="Internal").ap()
    k_dram = nc.dram_tensor("k_parts", [2 * PARTS - 1, HD * H, N], BF16, kind="Internal").ap()
    ctx = ExitStack()
    with ctx:
        def sb(name, shape, dt=F32):
            return ctx.enter_context(nc.sbuf_tensor(name, shape, dt))

        def pb(name, shape):
            return ctx.enter_context(nc.psum_tensor(name, shape, F32))

        def sem(name):
            return ctx.enter_context(nc.semaphore(name))

        ident = sb("ident", [128, 128])
        pick_prev = sb("pick_prev", [128, W], U32)
        alibi_own = sb("alibi_own", [128, G, W])
        alibi_prev = sb("alibi_prev", [128, G, W])
        q_bias = sb("q_bias", [128, 1])
        ramp = sb("ramp", [128, E])
        masked = sb("masked", [128, G, W])
        wqkv = sb("wqkv", [128, 3 * C])
        bqkv = sb("bqkv", [128, 3])
        wp = sb("wp", [128, C])
        pbias = sb("pbias", [128, C])
        gbias = sb("gbias", [E, 1])
        WW = E * FF + FF
        wg_hi, wg_lo = sb("wg_hi", [128, WW], F32R), sb("wg_lo", [128, WW], F32R)
        wu_hi, wu_lo = sb("wu_hi", [128, WW], F32R), sb("wu_lo", [128, WW], F32R)
        gw = sb("gw", [128, E])
        gw_hi, gw_lo = sb("gw_hi", [128, E], F32R), sb("gw_lo", [128, E], F32R)
        wd = sb("wd", [128, E // 2, C])
        wd_sh = sb("wd_sh", [FF, C])

        xin = sb("xin", [128, T, C])
        xtin = sb("xtin", [128, N])
        xtv = sb("xtv", [128, N])
        xb = sb("xb", [128, T, C])
        qk = sb("qk", [128, 2, N])
        rest = sb("rest", [128, 2, N])
        parts = sb("parts", [128, PARTS, 2, N], BF16)
        q_stack = sb("q_stack", [ROWS, H, N], BF16)
        k_stack = sb("k_stack", [ROWS, H, N], BF16)
        vbd = sb("vbd", [128, SB, G, HG, HD + 1])
        sf = sb("sf", [128, 2, G, SBT, W])
        mx = sb("mx", [128, 2, G * SBT])
        px = sb("px", [128, 2, G * SBT * W])
        pt = sb("pt", [128, 2, G, SBT, W])
        p_own = sb("p_own", [128, 2, G, SBT, W])
        p_prev = sb("p_prev", [128, 2, G, SBT, W])
        rden = sb("rden", [128, H])
        on = sb("on", [128, T, H, HD])
        ot = sb("ot", [128, N])
        y1 = sb("y1", [128, T, C])
        x1 = sb("x1", [128, T, C])
        x1r = sb("x1r", [128, T, C])
        xh, xl = sb("xh", [128, N], F32R), sb("xl", [128, N], F32R)
        lt = sb("lt", [E, N])
        rt = sb("rt", [128, 9, T, E])
        rs = sb("rs", [128, 6, T])
        gt = sb("gt", [E, N])
        gate_rows = sb("gate_rows", [128, E // 2, N])
        th = sb("th", [128, 2, N])
        ga = sb("ga", [128, 2, N])
        hid = sb("hid", [128, NC_, N])
        wg, wu = (hid[:, :, :].rearrange("p c n -> p (c n)")[:, n * WW:(n + 1) * WW] for n in range(2))
        stats = sb("stats", [128, T, 6])
        mv1, mv2 = sb("mv1", [128, T, 2]), sb("mv2", [128, T, 2])
        rstd1, rstd2 = sb("rstd1", [128, T]), sb("rstd2", [128, T])
        shift2 = sb("shift2", [128, T])
        minus_half = sb("minus_half", [128, T])
        y2 = sb("y2", [128, T, C])
        ob = sb("ob", [128, T, C])

        sc = pb("sc", [128, G, SBT, 2 * W])
        bank = pb("bank", [128, N])
        pv = bank[:, 0:H * (HD + 1)].rearrange("p (h d) -> p h d", d=HD + 1)
        logits = bank[:, N - T * E:N].rearrange("p (t e) -> p t e", e=E)
        m0, m1 = pb("m0", [128, N]), pb("m1", [128, N])
        pg, pu = pb("pg", [128, N]), pb("pu", [128, N])
        pd = pb("pd", [128, T, C])

        qkv_in = sem("qkv_in")
        const_in = sem("const_in")
        const_dve = sem("const_dve")
        const_pool = sem("const_pool")
        const_act = sem("const_act")
        xt_in = sem("xt_in")
        x_in = sem("x_in")
        xb_done = sem("xb_done")
        q_mm, q_out = sem("q_mm"), sem("q_out")
        rest_done = sem("rest_done")
        part0_done, part1_done, part2_done = sem("part0_done"), sem("part1_done"), sem("part2_done")
        parts_out = sem("parts_out")
        stack_in = sem("stack_in")
        k_mm, k_out = sem("k_mm"), sem("k_out")
        v_mm, v_out = sem("v_mm"), sem("v_out")
        sc_mm = sem("sc_mm")
        own_out = sem("own_out")
        fold_done = sem("fold_done")
        max_done = sem("max_done")
        sub_done = sem("sub_done")
        exp_done = sem("exp_done")
        pt_done = sem("pt_done")
        own_done = sem("own_done")
        prev_done = sem("prev_done")
        pv_mm = sem("pv_mm")
        rden_done = sem("rden_done")
        on_done = sem("on_done")
        ot_mm, ot_out = sem("ot_mm"), sem("ot_out")
        y_mm, y_out = sem("y_mm"), sem("y_out")
        ln1 = sem("ln1")
        rstd1_done, rstd2_done = sem("rstd1_done"), sem("rstd2_done")
        x1t_mm = sem("x1t_mm")
        xh_out, xl_out = sem("xh_out"), sem("xl_out")
        x1r_done = sem("x1r_done")
        lg_mm, lg_out = sem("lg_mm"), sem("lg_out")
        logit_mm, ez_out = sem("logit_mm"), sem("ez_out")
        route = sem("route")
        gt_mm, gt_out = sem("gt_mm"), sem("gt_out")
        gates_out = sem("gates_out")
        gates_in = (sem("gates_in_first"), sem("gates_in_second"))
        gate_mm, up_mm = sem("gate_mm"), sem("up_mm")
        tanh_out = sem("tanh_out")
        ga_done = sem("ga_done")
        hid_done = sem("hid_done")
        gated = sem("gated")
        down_mm = sem("down_mm")
        y2_done = sem("y2_done")
        ln2 = sem("ln2")
        ob_done = sem("ob_done")
        out_dma = sem("out_dma")

        X_IN = 16 * 2
        CONST_IN = 16 * 13
        PARTS_OUT = 16 * 3
        STACK = 16 * 2 * PARTS
        block = ctx.enter_context(nc.Block())

        def apart(eng):
            eng.nop(nofuse=True)

        def is_first(b):
            return isinstance(b, int) and b == 0

        def turns(eng, work, start_up):
            work(None, None, None, 0)
            start_up()
            work(None, None, 0, 1)
            work(None, 0, 1, 2)
            with eng.Fori(1, B - 2) as i:
                work(i - 1, i, i + 1, i + 2)
            work(B - 3, B - 2, B - 1, None)
            work(B - 2, B - 1, None, None)
            work(B - 1, None, None, None)

        @block.sync
        def _(sp):
            for dst, src in ((wqkv[:, :], wqkv_t), (bqkv[:, :], qkv_b)):
                sp.dma_start(dst, src).then_inc(qkv_in, 16)

            def batch_of(dram, b):
                return dram[b, :, :] if isinstance(b, int) else dram[bass.ds(b, 1), :, :].rearrange("b r c -> (b r) c")

            def load_xt(b):
                if not is_first(b):
                    sp.wait_ge(k_mm, b)
                    apart(sp)
                sp.dma_start(xtin[:, :], batch_of(xt, b)).then_inc(xt_in, 16)

            def load_x(b):
                if not is_first(b):
                    sp.wait_ge(v_mm, b)
                    apart(sp)
                    sp.wait_ge(xb_done, b)
                    apart(sp)
                sp.dma_start(xtv[:, :], batch_of(xt, b)).then_inc(x_in, 16)
                sp.dma_start(xin[:, :, :], batch_of(x, b).rearrange("(t p) d -> p t d", p=128)).then_inc(x_in, 16)

            load_xt(0)
            load_x(0)
            for dst, src in ((ident[:, :], ident_in), (pick_prev[:, :], pick_in),
                             (alibi_own[:, :, :], own_in.rearrange("p (g w) -> p g w", g=G)),
                             (alibi_prev[:, :, :], prev_in.rearrange("p (g w) -> p g w", g=G)),
                             (pbias[:, :], proj_b.rearrange("(a n) -> a n", a=1).broadcast_to([128, C])),
                             (wp[:, :], wp_t), (gw[:, :], gate_w),
                             (gbias[:, :], gate_b.rearrange("(n a) -> n a", a=1)), (ramp[:, :], ramp_in)):
                sp.dma_start(dst, src).then_inc(const_in, 16)

            for dst, src in ((wg, w_gate), (wu, w_up), (wd[:, :, :], w_down.rearrange("p (c d) -> p c d", d=C)),
                             (wd_sh[:, :], w_down_sh)):
                sp.dma_start(dst, src).then_inc(const_in, 16)

            def spread_gates(b):
                sp.wait_ge(gt_out, b + 1)
                apart(sp)
                if not is_first(b):
                    for half in gates_in:
                        sp.wait_ge(half, 32 * b)
                        apart(sp)
                    sp.wait_ge(gated, (NC_ - 1) * b)
                    apart(sp)
                sp.dma_start(gates_dram, gt[:, :]).then_inc(gates_out, 16)
                sp.wait_ge(gates_out, 16 * b + 16)
                apart(sp)
                for half in range(2):
                    c = half * E // 4
                    for e in range(2):
                        sp.dma_start(gate_rows[FF * e:FF * (e + 1), c:c + E // 4, :],
                                     gates_dram.rearrange("(c e) n -> e c n", e=2)[e:e + 1, c:c + E // 4, :]
                                     .broadcast_to([FF, E // 4, N])).then_inc(gates_in[half], 16)

            def store(b):
                sp.wait_ge(ob_done, b + 1)
                apart(sp)
                sp.dma_start(batch_of(out, b).rearrange("(t p) d -> p t d", p=128), ob[:, :, :]).then_inc(out_dma, 16)

            def store_parts(b):
                if not is_first(b):
                    sp.wait_ge(stack_in, STACK * b)
                    apart(sp)
                sp.wait_ge(part2_done, b + 1)
                apart(sp)
                for dram, n in ((q_dram, PARTS), (k_dram[0:PARTS], PARTS), (k_dram[PARTS:], PARTS - 1)):
                    sp.dma_start(dram.rearrange("n p t -> p n t"), parts[:, 0:n, 0 if dram is q_dram else 1, :])\
                        .then_inc(parts_out, 16)

            def stack(b):
                sp.wait_ge(parts_out, PARTS_OUT * b + PARTS_OUT)
                apart(sp)
                if not is_first(b):
                    sp.wait_ge(sc_mm, 4 * b)
                    apart(sp)
                one = PARTS * HD
                q_rows, k_rows = (dram.rearrange("n (d h) t -> (n d) (h t)", h=H) for dram in (q_dram, k_dram))
                for n in range(PARTS):
                    for dst, src in ((q_stack, q_rows[0:one, :]), (k_stack, k_rows[n * HD:n * HD + one, :])):
                        sp.dma_start(dst[n * one:(n + 1) * one, :, :].rearrange("p h t -> p (h t)"), src)\
                            .then_inc(stack_in, 16)

            store_parts(0)
            load_xt(1)
            stack(0)
            load_x(1)
            store_parts(1)
            load_xt(2)
            stack(1)
            load_x(2)
            spread_gates(0)
            store_parts(2)
            load_xt(3)
            stack(2)
            load_x(3)
            with sp.Fori(1, B - 3) as i:
                spread_gates(i)
                store_parts(i + 2)
                load_xt(i + 3)
                stack(i + 2)
                store(i - 1)
                load_x(i + 3)
            spread_gates(B - 3)
            store_parts(B - 1)
            stack(B - 1)
            store(B - 4)
            for b in (B - 2, B - 1):
                spread_gates(b)
                store(b - 1)
            store(B - 1)
            sp.wait_ge(out_dma, 16 * B)
            apart(sp)

        @block.gpsimd
        def _(pool):
            pool.memset(vbd[:, :, :, :, :], 0.0).then_inc(const_pool, 1)
            pool.memset(masked[:, :, :], MASKED).then_inc(const_pool, 1)
            pool.memset(minus_half[:, :], -0.5).then_inc(const_pool, 1)
            pool.wait_ge(const_pool, 3)
            for h in range(HG):
                pool.memset(vbd[W * h:W * (h + 1), :, :, h, HD:HD + 1].rearrange("p s g a -> p (s g) a"), 1.0)\
                    .then_inc(const_pool, 1)

            def start_up():
                pool.wait_ge(const_in, CONST_IN)

            def work(bo, bf, ba, bp):
                for step in steps("POOL", bo, bf, ba, bp):
                    first, first_pre = is_first(ba), is_first(bp)
                    if step[0] == "xb":
                        pool.wait_ge(x_in, X_IN * bp + X_IN)
                        if first_pre:
                            pool.wait_ge(const_in, CONST_IN)
                        else:
                            pool.wait_ge(y_out, bp)
                        pool.tensor_tensor(xb[:, :, :], xin[:, :, :],
                                           pbias[:, :].rearrange("p (a d) -> p a d", a=1).broadcast_to([128, T, C]),
                                           ALU.add).then_inc(xb_done, 1)
                    elif step[0] == "scores":
                        t = step[1]
                        pool.wait_ge(max_done, 4 * ba + t + 1)
                        flat = sf[:, t % 2].rearrange("p g s w -> p (g s) w")
                        pool.tensor_tensor(flat, flat, mx[:, t % 2, :].rearrange("p (a w) -> p a w", w=1)
                                           .broadcast_to([128, G * SBT, W]), ALU.subtract).then_inc(sub_done, 1)
                    elif step[0] == "exp":
                        t = step[1]
                        pool.wait_ge(pt_done, 4 * ba + t + 1)
                        if not (first and t < 2):
                            pool.wait_ge(pv_mm, 4 * ba + t - 1)
                        pool.tensor_tensor(p_prev[:, t % 2], pt[:, t % 2],
                                           alibi_prev[:, :, :].rearrange("p g (a w) -> p g a w", a=1)
                                           .broadcast_to([128, G, SBT, W]), ALU.mult).then_inc(prev_done, 1)
                    elif step[0] == "part0":
                        pool.wait_ge(part0_done, bp + 1)
                        pool.tensor_tensor(rest[:, :, :], qk[:, :, :], parts[:, 0], ALU.subtract).then_inc(rest_done, 1)
                    elif step[0] == "split":
                        pool.wait_ge(part1_done, bp + 1)
                        pool.tensor_tensor(parts[:, 2], rest[:, :, :], parts[:, 1], ALU.subtract).then_inc(part2_done, 1)
                    elif step[0] == "gate":
                        j = step[1]
                        pool.wait_ge(gates_in[0 if j <= E // 4 else 1], 32 * bf + 32)
                        pool.wait_ge(hid_done, NC_ * bf + j + 1)
                        pool.tensor_tensor(hid[:, j, :], hid[:, j, :], gate_rows[:, j - 1, :],
                                           ALU.mult).then_inc(gated, 1)

                    elif step[0] == "proj":
                        pool.wait_ge(ln1, 4 * ba + 3)
                        pool.tensor_tensor(rstd1[:, :], rstd1[:, :], minus_half[:, :], ALU.pow).then_inc(rstd1_done, 1)
                    elif step[0] == "norm":
                        pool.wait_ge(ln2, 4 * bo + 4)
                        pool.tensor_tensor(rstd2[:, :], rstd2[:, :], minus_half[:, :], ALU.pow).then_inc(rstd2_done, 1)
                        pool.wait_ge(rstd2_done, 2 * bo + 1)
                        pool.tensor_tensor(shift2[:, :], shift2[:, :], rstd2[:, :], ALU.mult).then_inc(rstd2_done, 1)

            turns(pool, work, start_up)

        @block.scalar
        def _(act):
            act.wait_ge(qkv_in, 32)
            act.wait_ge(const_dve, 1)
            act.wait_ge(const_pool, 7)

            def start_up():
                act.wait_ge(const_in, CONST_IN)
                act.activation(gw_hi[:, :], gw[:, :], ACT.Copy).then_inc(const_act, 1)
                act.activation(wg_hi[:, :], wg, ACT.Copy).then_inc(const_act, 1)
                act.activation(wu_hi[:, :], wu, ACT.Copy).then_inc(const_act, 1)

            def work(bo, bf, ba, bp):
                for step in steps("ACT", bo, bf, ba, bp):
                    first, first_pre = is_first(ba), is_first(bp)
                    kind = step[0]
                    if kind == "silu":
                        j = step[1]
                        rows = FF if j == 0 else 128
                        act.wait_ge(gate_mm, NC_ * bf + j + 1)
                        act.activation(th[0:rows, j % 2, :], pg[0:rows, :], ACT.Tanh, scale=0.5).then_inc(tanh_out, 1)
                    elif kind == "logits":
                        act.wait_ge(lg_mm, bf + 1)
                        act.activation(lt[:, :], m1[0:E, :], ACT.Identity, bias=gbias[:, 0:1]).then_inc(lg_out, 1)
                    elif kind == "logits_t":
                        act.wait_ge(logit_mm, bf + 1)
                        act.activation(rt[:, 0, :, :], logits, ACT.Exp, scale=-1.0).then_inc(ez_out, 1)
                    elif kind == "keep":
                        act.wait_ge(ln1, 4 * bf + 4)
                        if not is_first(bf):
                            act.wait_ge(y2_done, bf)
                        act.activation(x1r[:, :, :], x1[:, :, :], ACT.Copy, scale=2.0).then_inc(x1r_done, 1)
                    elif kind == "gates_t":
                        act.wait_ge(gt_mm, bf + 1)
                        if not (is_first(bf)):
                            act.wait_ge(gates_out, 16 * bf)
                        act.activation(gt[:, :], m1[0:E, :], ACT.Copy).then_inc(gt_out, 1)
                    elif kind == "qk":
                        act.wait_ge(q_mm, bp + 1)
                        if not first_pre:
                            act.wait_ge(rest_done, bp)
                        act.activation(qk[:, 0, :], m0[:, :], ACT.Identity, bias=q_bias[:, 0:1],
                                       scale=SCALE).then_inc(q_out, 1)
                        act.wait_ge(k_mm, bp + 1)
                        act.activation(qk[:, 1, :], m1[:, :], ACT.Identity, bias=bqkv[:, 1:2]).then_inc(k_out, 1)
                    elif kind == "part0":
                        act.wait_ge(q_out, bp + 1)
                        act.wait_ge(k_out, bp + 1)
                        if not first_pre:
                            act.wait_ge(parts_out, PARTS_OUT * bp)
                        act.activation(parts[:, 0], qk[:, :, :], ACT.Copy).then_inc(part0_done, 1)
                    elif kind == "split":
                        act.wait_ge(rest_done, bp + 1)
                        act.activation(parts[:, 1], rest[:, :, :], ACT.Copy).then_inc(part1_done, 1)
                    elif kind == "scores":
                        t = step[1]
                        act.wait_ge(sc_mm, 4 * ba + t + 1)
                        act.activation(sf[:, t % 2], sc[:, :, :, W:2 * W], ACT.Copy).then_inc(own_out, 1)
                    elif kind == "exp":
                        t = step[1]
                        act.wait_ge(sub_done, 4 * ba + t + 1)
                        act.activation(px[:, t % 2, :], sf[:, t % 2].rearrange("p g s w -> p (g s w)"),
                                       ACT.Exp).then_inc(exp_done, 1)
                    elif kind == "heads_t":
                        act.wait_ge(ot_mm, ba + 1)
                        act.activation(ot[:, :], m0[:, :], ACT.Identity, bias=bqkv[:, 2:3]).then_inc(ot_out, 1)
                    elif kind == "v":
                        h = step[1]
                        act.wait_ge(v_mm, bp + 1)
                        if ba is not None and h == 0:
                            act.wait_ge(pv_mm, 4 * bp)
                        for s in range(SBT):
                            last = act.activation(
                                vbd[W * h:W * (h + 1), :, :, h, 0:HD].rearrange("p (t s) g d -> p t s g d", s=SBT)[:, :, s],
                                m1[W * s:W * (s + 1), :].rearrange("p (t g h d) -> p t g h d", t=T, h=HG, d=HD)[:, :, :, h],
                                ACT.Copy)
                        last.then_inc(v_out, 1)
                    elif kind == "store":
                        act.wait_ge(rstd2_done, 2 * bo + 2)
                        if not is_first(bo):
                            act.wait_ge(out_dma, 16 * bo)
                        for t in range(T):
                            last = act.activation(ob[:, t, :], y2[:, t, :], ACT.Identity, scale=rstd2[:, t:t + 1],
                                                  bias=shift2[:, t:t + 1])
                        last.then_inc(ob_done, 1)
                    elif kind == "x1_t":
                        act.wait_ge(x1t_mm, ba + 1)
                        act.activation(xh[:, :], m0[:, :], ACT.Copy).then_inc(xh_out, 1)

            turns(act, work, start_up)

        @block.vector
        def _(dve):
            dve.wait_ge(qkv_in, 32)
            dve.tensor_scalar(q_bias[:, :], bqkv[:, 0:1], SCALE, None, ALU.mult).then_inc(const_dve, 1)

            def start_up():
                dve.wait_ge(const_in, CONST_IN)
                dve.wait_ge(const_pool, 7)
                for n, (lo, w, hi) in enumerate(((gw_lo, gw[:, :], gw_hi), (wg_lo, wg, wg_hi), (wu_lo, wu, wu_hi))):
                    dve.wait_ge(const_act, n + 1)
                    dve.tensor_tensor(lo[:, :], w, hi[:, :].bitcast(F32), ALU.subtract).then_inc(const_dve, 1)

            def chain(s, per, b, first=0):
                done = [first]

                def link(ins, alone=False):
                    done[0] += 1
                    ins.then_inc(s, 1)
                    dve.wait_ge(s, per * b + done[0])
                    if alone:
                        apart(dve)
                return link

            def mean_and_variance(link, src, mv, var):
                for t in range(T):
                    last = dve.bn_stats(stats[:, t, :], src[:, t, :])
                link(last, alone=True)
                for t in range(T):
                    last = dve.bn_aggr(mv[:, t, :], stats[:, t, :])
                link(last)
                link(dve.tensor_scalar(var[:, :], mv[:, :, 1], EPS, None, ALU.add))

            def per_token(v):
                return v.rearrange("p (t a) -> p t a", a=1).broadcast_to([128, T, E])

            def router(b, part):
                link = chain(route, 16, b, first=4 * part)
                e, v, eq, key, s1, v2, s2, sel, gates = (rt[:, n] for n in range(9))
                m1_, k1, m2, k2, den, rd = (rs[:, n] for n in range(6))
                ramps = ramp[:, :].rearrange("p (a e) -> p a e", a=1).broadcast_to([128, T, E])
                if part == 0:
                    link(dve.tensor_scalar(e, e, 1.0, None, ALU.add))
                    link(dve.reciprocal(v, e))
                    link(dve.tensor_reduce(m1_, v, AX.X, ALU.max))
                    link(dve.tensor_tensor(eq, v, per_token(m1_), ALU.is_equal))
                elif part == 1:
                    link(dve.tensor_tensor(key, eq, ramps, ALU.mult))
                    link(dve.tensor_reduce(k1, key, AX.X, ALU.max))
                    link(dve.tensor_tensor(s1, key, per_token(k1), ALU.is_equal))
                    link(dve.scalar_tensor_tensor(out=v2, in0=s1, scalar=-2.0, in1=v, op0=ALU.mult, op1=ALU.add))
                elif part == 2:
                    link(dve.tensor_reduce(m2, v2, AX.X, ALU.max))
                    link(dve.tensor_tensor(eq, v2, per_token(m2), ALU.is_equal))
                    link(dve.tensor_tensor(key, eq, ramps, ALU.mult))
                    link(dve.tensor_reduce(k2, key, AX.X, ALU.max))
                else:
                    link(dve.tensor_tensor(s2, key, per_token(k2), ALU.is_equal))
                    dve.tensor_tensor(den, m1_, m2, ALU.add)
                    link(dve.tensor_tensor(sel, s1, s2, ALU.add))
                    dve.reciprocal(rd, den)
                    link(dve.tensor_tensor(eq, sel, v, ALU.mult))
                    link(dve.tensor_tensor(gates, eq, per_token(rd), ALU.mult))

            def work(bo, bf, ba, bp):
                for step in steps("DVE", bo, bf, ba, bp):
                    first = is_first(ba)
                    kind = step[0]
                    if kind == "silu":
                        j = step[1]
                        rows = FF if j == 0 else 128
                        dve.wait_ge(tanh_out, NC_ * bf + j + 1)
                        if j > 1:
                            dve.wait_ge(hid_done, NC_ * bf + j - 1)
                        elif j == 0 and not is_first(bf):
                            dve.wait_ge(hid_done, NC_ * bf)
                        dve.scalar_tensor_tensor(out=ga[0:rows, j % 2, :], in0=th[0:rows, j % 2, :], scalar=1.0,
                                                 in1=pg[0:rows, :], op0=ALU.add, op1=ALU.mult).then_inc(ga_done, 1)
                    elif kind == "up":
                        j = step[1]
                        rows = FF if j == 0 else 128
                        dve.wait_ge(ga_done, NC_ * bf + j + 1)
                        dve.wait_ge(up_mm, NC_ * bf + j + 1)
                        dve.scalar_tensor_tensor(out=hid[0:rows, j, :], in0=ga[0:rows, j % 2, :], scalar=0.5,
                                                 in1=pu[0:rows, :], op0=ALU.mult, op1=ALU.mult).then_inc(hid_done, 1)
                    elif kind == "router":
                        dve.wait_ge(ez_out, bf + 1)
                        router(bf, step[1])
                    elif kind == "scores":
                        t = step[1]
                        dve.wait_ge(own_out, 4 * ba + t + 1)
                        apart(dve)
                        picks = pick_prev[:, :].rearrange("p (a c w) -> p a c w", a=1, c=1)
                        s0 = 1 if t == 0 else 0
                        if t == 0:
                            dve.copy_predicated(sf[:, 0, :, 0, :],
                                                pick_prev[:, :].rearrange("p (a w) -> p a w", a=1).broadcast_to([128, G, W]),
                                                masked[:, :, :])
                        dve.copy_predicated(sf[:, t % 2, :, s0:SBT, :], picks.broadcast_to([128, G, SBT - s0, W]),
                                            sc[:, :, s0:SBT, 0:W]).then_inc(fold_done, 1)
                        dve.wait_ge(fold_done, 4 * ba + t + 1)
                        flat = sf[:, t % 2].rearrange("p g s w -> p (g s) w")
                        dve.tensor_reduce(mx[:, t % 2, :], flat, AX.X, ALU.max).then_inc(max_done, 1)
                    elif kind == "exp":
                        t = step[1]
                        dve.wait_ge(exp_done, 4 * ba + t + 1)
                        if not (first and t < 2):
                            dve.wait_ge(prev_done, 4 * ba + t - 1)
                        dve.transpose(pt[:, t % 2].rearrange("p g s w -> p (g s w)"), px[:, t % 2, :]).then_inc(pt_done, 1)
                        dve.wait_ge(pt_done, 4 * ba + t + 1)
                        if not (first and t < 2):
                            dve.wait_ge(pv_mm, 4 * ba + t - 1)
                        dve.tensor_tensor(p_own[:, t % 2], pt[:, t % 2],
                                          alibi_own[:, :, :].rearrange("p g (a w) -> p g a w", a=1)
                                          .broadcast_to([128, G, SBT, W]), ALU.mult).then_inc(own_done, 1)
                    elif kind == "pv":
                        t = step[1]
                        dve.wait_ge(pv_mm, 4 * ba + t + 1)
                        dve.reciprocal(rden[:, :], pv[:, :, HD]).then_inc(rden_done, 1)
                        dve.wait_ge(rden_done, 4 * ba + t + 1)
                        dve.tensor_tensor(on[:, t, :, :], pv[:, :, 0:HD],
                                          rden[:, :].rearrange("p (h a) -> p h a", a=1).broadcast_to([128, H, HD]),
                                          ALU.mult).then_inc(on_done, 1)
                    elif kind == "proj":
                        dve.wait_ge(y_mm, ba + 1)
                        dve.wait_ge(xb_done, ba + 1)
                        dve.tensor_tensor(y1[:, :, :], m1[:, :].rearrange("p (t d) -> p t d", t=T), xb[:, :, :],
                                          ALU.add).then_inc(y_out, 1)
                        dve.wait_ge(y_out, ba + 1)
                        mean_and_variance(chain(ln1, 4, ba), y1, mv1, rstd1)
                    elif kind == "x1":
                        if not first:
                            dve.wait_ge(x1r_done, ba)
                        dve.wait_ge(rstd1_done, ba + 1)
                        for t in range(T):
                            last = dve.tensor_scalar(x1[:, t, :], y1[:, t, :], mv1[:, t, 0:1], rstd1[:, t:t + 1],
                                                     ALU.subtract, ALU.mult)
                        last.then_inc(ln1, 1)
                    elif kind == "x1_t":
                        dve.wait_ge(xh_out, ba + 1)
                        dve.tensor_tensor(xl[:, :], m0[:, :], xh[:, :].bitcast(F32), ALU.subtract).then_inc(xl_out, 1)
                    elif kind == "residual":
                        dve.wait_ge(down_mm, NC_ * bo + NC_)
                        dve.wait_ge(x1r_done, bo + 1)
                        if not is_first(bo):
                            dve.wait_ge(ob_done, bo)
                        dve.tensor_tensor(y2[:, :, :], x1r[:, :, :], pd[:, :, :], ALU.add).then_inc(y2_done, 1)
                    elif kind == "norm":
                        dve.wait_ge(y2_done, bo + 1)
                        link = chain(ln2, 4, bo)
                        mean_and_variance(link, y2, mv2, rstd2)
                        link(dve.tensor_scalar(shift2[:, :], mv2[:, :, 0], -1.0, None, ALU.mult))

            turns(dve, work, start_up)

        @block.tensor
        def _(pe):
            pe.wait_ge(qkv_in, 32)

            def start_up():
                pe.wait_ge(const_in, CONST_IN)
                pe.wait_ge(const_pool, 7)
                pe.wait_ge(const_dve, 4)

            def split_matmul(dst, w_hi, w_lo, start=True, stop=True):
                pe.matmul(dst, w_hi, xh[:, :], start=True, stop=False)
                pe.matmul(dst, w_hi, xl[:, :], start=False, stop=False)
                return pe.matmul(dst, w_lo, xh[:, :], start=False, stop=True)

            def work(bo, bf, ba, bp):
                for step in steps("PE", bo, bf, ba, bp):
                    first = is_first(ba)
                    kind = step[0]
                    if kind in ("gate_w", "up"):
                        j = step[1]
                        pe.wait_ge(xh_out, bf + 1)
                        pe.wait_ge(xl_out, bf + 1)
                        c0, c1 = (E * FF, E * FF + FF) if j == 0 else (128 * (j - 1), 128 * j)
                        if kind == "gate_w":
                            if not (is_first(bf) and j == 0):
                                pe.wait_ge(ga_done, NC_ * bf + j)
                            split_matmul(pg[0:c1 - c0, :], wg_hi[:, c0:c1], wg_lo[:, c0:c1]).then_inc(gate_mm, 1)
                        else:
                            if not (is_first(bf) and j == 0):
                                pe.wait_ge(hid_done, NC_ * bf + j)
                            split_matmul(pu[0:c1 - c0, :], wu_hi[:, c0:c1], wu_lo[:, c0:c1]).then_inc(up_mm, 1)
                    elif kind == "down":
                        j = step[1]
                        b = bf if j < LATE else bo
                        if j == 0:
                            pe.wait_ge(hid_done, NC_ * bf + 1)
                            if not (is_first(bf)):
                                pe.wait_ge(y2_done, bf)
                        else:
                            pe.wait_ge(gated, (NC_ - 1) * b + j)
                        rows = FF if j == 0 else 128
                        for t in range(T):
                            last = pe.matmul(pd[:, t, :], hid[0:rows, j, 128 * t:128 * (t + 1)],
                                             wd_sh[:, :] if j == 0 else wd[:, j - 1, :],
                                             start=(j == 0 and t == 0), stop=(j == NC_ - 1), skip_group_check=True)
                        last.then_inc(down_mm, 1)
                    elif kind == "logits":
                        pe.wait_ge(xh_out, bf + 1)
                        pe.wait_ge(xl_out, bf + 1)
                        if ba is not None:
                            pe.wait_ge(v_out, 4 * bf + 8)
                        split_matmul(m1[0:E, :], gw_hi[:, :], gw_lo[:, :]).then_inc(lg_mm, 1)
                    elif kind == "logits_t":
                        pe.wait_ge(lg_out, bf + 1)
                        pe.wait_ge(on_done, 4 * bf + 4)
                        apart(pe)
                        for t in range(T):
                            last = pe.transpose(logits[:, t, :], lt[:, 128 * t:128 * (t + 1)], ident[0:E, 0:E])
                        last.then_inc(logit_mm, 1)
                    elif kind == "gates_t":
                        pe.wait_ge(route, 16 * bf + 16)
                        if bp is not None:
                            pe.wait_ge(k_out, bp + 1)
                        for t in range(T):
                            last = pe.transpose(m1[0:E, 128 * t:128 * (t + 1)], rt[:, 8, t, :], ident[:, :])
                        last.then_inc(gt_mm, 1)
                    elif kind == "qk":
                        pe.wait_ge(xt_in, 16 * bp + 16)
                        if ba is not None:
                            pe.wait_ge(v_out, 4 * bp)
                        if bf is not None:
                            pe.wait_ge(xl_out, bf + 1)
                            pe.wait_ge(lg_out, bf + 1)
                        elif ba is not None:
                            pe.wait_ge(q_out, bp)
                        pe.matmul(m0[:, :], wqkv[:, 0:C], xtin[:, :], start=True, stop=True).then_inc(q_mm, 1)
                        pe.matmul(m1[:, :], wqkv[:, C:2 * C], xtin[:, :], start=True, stop=True).then_inc(k_mm, 1)
                    elif kind == "v":
                        pe.wait_ge(x_in, X_IN * bp + X_IN)
                        if ba is not None:
                            pe.wait_ge(y_out, ba + 1)
                        else:
                            pe.wait_ge(k_out, bp + 1)
                        for t in range(T):
                            last = pe.matmul(m1[:, 128 * t:128 * (t + 1)], xtv[:, 128 * t:128 * (t + 1)],
                                             wqkv[:, 2 * C:3 * C], start=True, stop=True)
                        last.then_inc(v_mm, 1)
                    elif kind == "scores":
                        t = step[1]
                        pe.wait_ge(stack_in, STACK * ba + STACK)
                        if not (first and t == 0):
                            pe.wait_ge(fold_done, 4 * ba + t)
                        for g in range(G):
                            for s in range(SBT):
                                n = SBT * t + s
                                k0 = W if n == 0 else 0
                                for h in range(HG):
                                    last = pe.matmul(sc[W * h:W * (h + 1), g, s, k0:2 * W],
                                                     q_stack[:, HG * g + h, W * n:W * (n + 1)],
                                                     k_stack[:, HG * g + h, W * (n - 1) + k0:W * (n + 1)],
                                                     start=True, stop=True, tile_position=(0, W * h))
                        last.then_inc(sc_mm, 1)
                    elif kind == "pv":
                        t = step[1]
                        pe.wait_ge(own_done, 4 * ba + t + 1)
                        pe.wait_ge(prev_done, 4 * ba + t + 1)
                        if t == 0:
                            pe.wait_ge(v_out, 4 * ba + 4)
                        if not (first and t == 0):
                            pe.wait_ge(on_done, 4 * ba + t)
                        if t == 0 and bf is not None:
                            pe.wait_ge(ez_out, bf + 1)
                        for s in range(SBT):
                            b_ = SBT * t + s
                            for g in range(G):
                                dst = pv[W * s:W * (s + 1), HG * g:HG * (g + 1), :].rearrange("p h d -> p (h d)")
                                last = pe.matmul(dst, p_own[:, t % 2, g, s, :],
                                                 vbd[:, b_, g].rearrange("p h d -> p (h d)"),
                                                 start=True, stop=(b_ == 0), tile_position=(0, W * s))
                                if b_ > 0:
                                    last = pe.matmul(dst, p_prev[:, t % 2, g, s, :],
                                                     vbd[:, b_ - 1, g].rearrange("p h d -> p (h d)"),
                                                     start=False, stop=True, tile_position=(0, W * s))
                        last.then_inc(pv_mm, 1)
                    elif kind == "heads_t":
                        pe.wait_ge(on_done, 4 * ba + 4)
                        if bp is not None:
                            pe.wait_ge(q_out, bp + 1)
                        for t in range(T):
                            last = pe.transpose(m0[:, 128 * t:128 * (t + 1)],
                                                on[:, t].rearrange("p h d -> p (h d)"), ident[:, :])
                        last.then_inc(ot_mm, 1)
                    elif kind == "proj":
                        pe.wait_ge(ot_out, ba + 1)
                        if bf is not None:
                            pe.wait_ge(gt_out, bf + 1)
                        elif bp is not None:
                            pe.wait_ge(k_out, bp + 1)
                        for t in range(T):
                            last = pe.matmul(m1[:, 128 * t:128 * (t + 1)], ot[:, 128 * t:128 * (t + 1)], wp[:, :],
                                             start=True, stop=True)
                        last.then_inc(y_mm, 1)
                    elif kind == "x1_t":
                        pe.wait_ge(ln1, 4 * ba + 4)
                        for t in range(T):
                            last = pe.transpose(m0[:, 128 * t:128 * (t + 1)], x1[:, t, :], ident[:, :])
                        last.then_inc(x1t_mm, 1)

            turns(pe, work, start_up)


def constants():
    p = np.arange(128)
    ident = np.eye(128, dtype=np.float32)
    pick = (np.arange(W)[None, :] > (p[:, None] % W)).astype(np.uint32)
    slopes = (2.0 ** -0.5) ** np.arange(1, H + 1)
    head = np.arange(G)[None, :, None] * HG + (p // W)[:, None, None]
    key = (p % W)[:, None, None]
    q = np.arange(W)[None, None, :]
    own = np.where(key <= q, np.exp(slopes[head] * (key - q)), 0.0)
    prev = np.where(key > q, np.exp(slopes[head] * (key - W - q)), 0.0)
    ramp = np.broadcast_to(E - np.arange(E, dtype=np.float32), (128, E))
    f = lambda a: np.ascontiguousarray(a.reshape(128, -1).astype(np.float32))
    return dict(ident=ident, pick=pick, own=f(own), prev=f(prev), ramp=f(ramp))


def kernel(**inputs):
    import concourse.bacc as bacc
    from concourse.bass_utils import run_bass_kernel_spmd

    a = {k.replace("L0_", ""): np.asarray(v) for k, v in inputs.items()}
    c = np.ascontiguousarray

    def experts(routed, shared):
        return c(np.concatenate([routed.transpose(1, 0, 2).reshape(C, E * FF), shared], axis=1))

    def qkv_rows(w):
        q_k = w[:2 * C].reshape(2, H, HD, -1).transpose(0, 2, 1, 3).reshape((2 * C,) + w.shape[1:])
        return np.concatenate([q_k, w[2 * C:]])

    data = dict(
        x=c(a["attn_x"]), xt=c(a["attn_x"].transpose(0, 2, 1)), wqkv_t=c(qkv_rows(a["attn_qkv_w"]).T),
        qkv_b=c(qkv_rows(a["attn_qkv_b"]).reshape(3, C).T), wp_t=c(a["attn_proj_w"].T), proj_b=c(a["attn_proj_b"]),
        gate_w=c(a["ffn_gate_w"]), gate_b=c(a["ffn_gate_b"]),
        w_gate=experts(a["ffn_experts_wg"], a["ffn_shared_wg"]),
        w_up=experts(a["ffn_experts_wu"], a["ffn_shared_wu"]),
        w_down=c(a["ffn_experts_wd"].reshape(E // 2, 128, C).transpose(1, 0, 2).reshape(128, -1)),
        w_down_sh=c(a["ffn_shared_wd"]))
    data.update(constants())

    nc = bacc.Bacc("TRN2", target_bir_lowering=False, num_devices=1)
    args = [nc.dram_tensor("in_" + k, v.shape, mybir.dt.from_np(v.dtype), kind="ExternalInput").ap()
            for k, v in data.items()]
    args.append(nc.dram_tensor("out", [B, N, C], F32, kind="ExternalOutput").ap())
    build(nc, *args)
    r = run_bass_kernel_spmd(nc, [{"in_" + k: v for k, v in data.items()}], core_ids=[0])
    return r.results[0]["out"]
```
